# Optimizing a Trainium2 kernel written in Bass

```python
import numpy as np
import jax
import jax.numpy as jnp

def _softmax(x, axis=-1):
    return jax.nn.softmax(x, axis=axis)

def _gelu(x):
    return jax.nn.gelu(x, approximate=True)

def _silu(x):
    return jax.nn.silu(x)

def _sigmoid(x):
    return jax.nn.sigmoid(x)

def _layernorm(x, axis=-1, eps=1e-05):
    m = jnp.mean(x, axis=axis, keepdims=True)
    v = jnp.var(x, axis=axis, keepdims=True)
    return (x - m) / jnp.sqrt(v + eps)

def _scatter_add(tgt, idx, src, axis=0):
    return tgt.at[idx].add(src)

def _segment_sum(src, seg, n):
    return jax.ops.segment_sum(src, seg, n)
kernel_name = 'mk_gnn_resnorm_d2_gnn_r8_1b270b'

def setup_inputs(seed: int=0):
    np.random.seed(seed)
    _w = jnp.asarray

    def _rec_inputs():
        import jax
        import jax.numpy as jnp
        _gk = jax.random.key(seed)
        x = -0.0001006 + 1 * jax.random.normal(jax.random.fold_in(_gk, 1), (12500, 48), jnp.float32)
        _s = jax.random.randint(jax.random.fold_in(_gk, 2), (100000,), 0, 12500, jnp.int32)
        _d = jax.random.randint(jax.random.fold_in(_gk, 3), (100000,), 0, 12500, jnp.int32)
        _loop = jnp.arange(12500, dtype=jnp.int32)
        src = jnp.concatenate([_s, _d, _loop])
        dst = jnp.concatenate([_d, _s, _loop])
        _o = jnp.argsort(dst, stable=True)
        src = src[_o]
        dst = dst[_o]
        edge_attr_48 = -4.21973e-05 + 0.999841 * jax.random.normal(jax.random.fold_in(_gk, 12), (212500, 48), jnp.float32)
        return (x, src, dst, edge_attr_48)
    x, src, dst, edge_attr_48 = _rec_inputs()

    def _L0_gnn_setup():
        import jax, jax.numpy as jnp
        import numpy as np
        N_NODES = 12500
        N_EDGES = 200000
        IN_FEAT = 48
        OUT_FEAT = 48
        key = jax.random.key(seed)
        k_h, k_src, k_dst, k_tw, k_tb, k_pw, k_pb = jax.random.split(key, 7)
        lim = 1.0 / np.sqrt(IN_FEAT)
        return {'h': jax.random.normal(k_h, (N_NODES, IN_FEAT), dtype=jnp.float32), 'theta_w': jax.random.uniform(k_tw, (OUT_FEAT, IN_FEAT), jnp.float32, -lim, lim), 'theta_b': jax.random.uniform(k_tb, (OUT_FEAT,), jnp.float32, -lim, lim), 'phi_w': jax.random.uniform(k_pw, (OUT_FEAT, IN_FEAT), jnp.float32, -lim, lim), 'phi_b': jax.random.uniform(k_pb, (OUT_FEAT,), jnp.float32, -lim, lim), 'src': jax.random.randint(k_src, (N_EDGES,), 0, N_NODES, dtype=jnp.int64), 'dst': jax.random.randint(k_dst, (N_EDGES,), 0, N_NODES, dtype=jnp.int64)}
    _L0_gnn_all = _L0_gnn_setup()
    _L0_gnn_in = {k: v for k, v in _L0_gnn_all.items() if k in ('theta_w', 'theta_b', 'phi_w', 'phi_b')}
    del _L0_gnn_all

    def _L1_gnn_setup():
        import jax, jax.numpy as jnp
        import numpy as np
        N_NODES = 12500
        N_EDGES = 200000
        D_FEAT = 48
        key = jax.random.key(seed)
        k1, k2, k3, k4 = jax.random.split(key, 4)
        node_feat = jax.random.normal(k1, (N_NODES, D_FEAT), dtype=jnp.float32)
        edge_feat = jax.random.normal(k2, (N_EDGES, D_FEAT), dtype=jnp.float32)
        src = jax.random.randint(k3, (N_EDGES,), 0, N_NODES, dtype=jnp.int32)
        dst = jax.random.randint(k4, (N_EDGES,), 0, N_NODES, dtype=jnp.int32)
        eps = jnp.zeros((1,), dtype=jnp.float32)
        return {'node_feat': node_feat, 'edge_feat': edge_feat, 'src': src, 'dst': dst, 'eps': eps}
    _L1_gnn_all = _L1_gnn_setup()
    _L1_gnn_in = {k: v for k, v in _L1_gnn_all.items() if k in ('eps',)}
    del _L1_gnn_all
    return {'x': x, 'src': src, 'dst': dst, 'edge_attr_48': edge_attr_48, 'L0_gnn_theta_w': _L0_gnn_in['theta_w'], 'L0_gnn_theta_b': _L0_gnn_in['theta_b'], 'L0_gnn_phi_w': _L0_gnn_in['phi_w'], 'L0_gnn_phi_b': _L0_gnn_in['phi_b'], 'L1_gnn_eps': _L1_gnn_in['eps']}

def reference(x, src, dst, edge_attr_48, L0_gnn_theta_w, L0_gnn_theta_b, L0_gnn_phi_w, L0_gnn_phi_b, L1_gnn_eps):
    import jax
    import jax.numpy as jnp

    def _L0_gnn_ref(h, theta_w, theta_b, phi_w, phi_b, src, dst):
        import jax, jax.numpy as jnp
        import numpy as np
        N_NODES = 12500
        N_EDGES = 200000
        IN_FEAT = 48
        OUT_FEAT = 48
        phi_all = h @ phi_w.T + phi_b
        diff = h[dst] - h[src]
        e = diff @ theta_w.T + theta_b + phi_all[src]
        out = jax.ops.segment_max(e, dst, num_segments=N_NODES)
        out = jnp.where(jnp.isneginf(out), 0.0, out)
        return out

    def _L1_gnn_ref(node_feat, edge_feat, src, dst, eps):
        import jax, jax.numpy as jnp
        import numpy as np
        N_NODES = 12500
        N_EDGES = 200000
        D_FEAT = 48
        m = jax.nn.relu(node_feat[src] + edge_feat)
        neigh = jax.ops.segment_sum(m, dst, num_segments=N_NODES)
        return (1.0 + eps[0]) * node_feat + neigh
    x = _layernorm(x + _L0_gnn_ref(x, L0_gnn_theta_w, L0_gnn_theta_b, L0_gnn_phi_w, L0_gnn_phi_b, src, dst), axis=-1)
    x = _layernorm(x + _L1_gnn_ref(x, edge_attr_48, src, dst, L1_gnn_eps), axis=-1)
    return x

_drawn_inputs = setup_inputs


def setup_inputs(seed=0):
    import zlib

    import numpy as np

    out = dict(_drawn_inputs(seed))
    spreads = {}
    factors = {}
    for name, (base, spread) in spreads.items():
        noise = np.random.default_rng([zlib.crc32(name.encode()), seed]).standard_normal(out[name].shape)
        drawn = base * np.exp(spread * noise) if base else spread * noise
        out[name] = jnp.asarray(drawn.astype(out[name].dtype))
    for name, factor in factors.items():
        out[name] = (out[name] * factor).astype(out[name].dtype)
    return out
```

```python
import concourse.bass as bass
from concourse import mybir
from contextlib import ExitStack


def gnn_resnorm(nc, x, src, dst, edge_attr, theta_w, theta_b, phi_w, phi_b, eps, out, shapes):
    fp32, bf16, i32 = mybir.dt.float32, mybir.dt.bfloat16, mybir.dt.int32
    ALU, ACT, AX = mybir.AluOpType, mybir.ActivationFunctionType, mybir.AxisListType

    N, D, E = shapes
    P = 128
    STEPS = -(-E // P)
    LAST = E - (P - 1) * STEPS
    T = 64
    PAIRS = LAST // (2 * T)
    MAIN = 2 * PAIRS
    TAIL = [T, STEPS - (MAIN + 1) * T]
    CHUNKS = MAIN + len(TAIL)
    assert 0 < TAIL[1] <= T and LAST > MAIN * T
    K = -(-N // P)
    NP = P * K
    NLAST = N - (P - 1) * K
    HI = NP // P
    B = 16
    BATCHES = T // B
    TAIL_STEPS = sum(TAIL)
    TAIL_BATCHES = [B] * (TAIL_STEPS // B) + ([TAIL_STEPS % B] if TAIL_STEPS % B else [])
    HUGE = 3.4028234e38
    EPS_LN = 1e-5
    NODE_GROUPS = [28, 28, 28, K - 84]
    GMAX = max(NODE_GROUPS)
    GROUP_AT = [sum(NODE_GROUPS[:g]) for g in range(len(NODE_GROUPS))]
    PAIR_TILES = K // 2
    assert K % 2 == 0
    PROD_GROUPS = [list(range(g, min(g + 4, PAIR_TILES))) for g in range(0, PAIR_TILES, 4)]
    C_PARTS = [0, 4, 8, len(PROD_GROUPS)]
    FULL_LOW, FULL_HIGH = slice(0, 112), slice(112, P - 1)

    c_dram = nc.dram_tensor("c_rows", [NP, D], fp32).ap()
    x1_dram = nc.dram_tensor("x1_rows", [NP, D], fp32).ap()
    scan_dram = nc.dram_tensor("scan_rows", [P * STEPS, D], fp32).ap()
    end_dram = nc.dram_tensor("last_edge", [HI, P], i32).ap()
    has_dram = nc.dram_tensor("has_edges", [HI, P], fp32).ap()
    c_tiles = c_dram.rearrange("(p k) d -> p k d", k=K)
    x1_tiles = x1_dram.rearrange("(p k) d -> p k d", k=K)
    scan_tiles = scan_dram.rearrange("(p t) d -> p (t d)", t=STEPS)
    end_tiles = end_dram.rearrange("h l -> (h l)").rearrange("(p k) -> p k", k=K)
    has_tiles = has_dram.rearrange("h l -> (h l)").rearrange("(p k) -> p k", k=K)
    x_full = x[0:(P - 1) * K, :].rearrange("(p k) d -> p k d", k=K)
    out_full = out[0:(P - 1) * K, :].rearrange("(p k) d -> p k d", k=K)
    edge_full = edge_attr[0:(P - 1) * STEPS, :].rearrange("(p t) d -> p (t d)", t=STEPS)
    edge_last = edge_attr[(P - 1) * STEPS:E, :].rearrange("(p t) d -> p (t d)", p=1)
    edge_all = bass.AP(tensor=edge_attr.tensor, offset=0, ap=[[STEPS * D, P], [1, LAST * D]])

    with ExitStack() as ctx:
        def sb(name, shape, dt):
            return ctx.enter_context(nc.sbuf_tensor(name, shape, dt))

        def pb(name, shape, dt=fp32):
            return ctx.enter_context(nc.psum_tensor(name, shape, dt))

        def sem(name):
            return ctx.enter_context(nc.semaphore(name))

        x_sb = sb("x_sb", [P, K, D], fp32)
        a_sb = sb("a_sb", [P, K, D], fp32)
        rows_sb = sb("rows_sb", [P, K, D], fp32)
        x1_sb = sb("x1_sb", [P, K, D], fp32)
        square = sb("square", [P, GMAX, D], fp32)
        end_sb = sb("end_sb", [P, K], i32)
        has_sb = sb("has_sb", [P, K], fp32)
        mean = sb("mean", [P, GMAX], fp32)
        rstd = sb("rstd", [P, GMAX], fp32)
        idx = sb("idx", [P, 2, T], i32)
        gath = sb("gath", [P, 2, T * D], fp32)
        edge = sb("edge", [P, 2, T * D], fp32)
        scan = sb("scan", [P, 2, T * D], fp32)
        dst_sb = sb("dst_sb", [P, STEPS], i32)
        keep = sb("keep", [P, STEPS], fp32)
        limit = sb("limit", [P, STEPS], fp32)
        dst_hi = sb("dst_hi", [P, STEPS], bf16)
        dst_lo = sb("dst_lo", [P, STEPS], bf16)
        scratch = edge[:, 0, 0:STEPS]
        scratch_i = scratch.bitcast(i32)
        hot_hi = sb("hot_hi", [P, 2, B, HI], bf16)
        hot_lo = sb("hot_lo", [P, 2, B, P], bf16)
        ident = sb("ident", [P, P], fp32)
        ones = sb("ones", [P, P], fp32)
        before = sb("before", [HI, HI], fp32)
        half = sb("half", [2 * D, 2], fp32)
        lane_i = sb("lane_i", [P, P], i32)
        lane = sb("lane", [P, P], bf16)
        zero_b = sb("zero_b", [P, P], bf16)
        part_end = sb("part_end", [P, 1], i32)
        eps_ln = sb("eps_ln", [P, 1], fp32)
        eps1 = sb("eps1", [P, 1], fp32)
        theta2 = sb("theta2", [D, 2, D], fp32)
        phi2 = sb("phi2", [D, 2, D], fp32)
        wt = sb("wt", [2 * D, 2, 2 * D], fp32)
        bias = sb("bias", [P, 2, D], fp32)
        xt = sb("xt", [2 * D, 2, 4 * P], fp32)
        prev = sb("prev", [P, 1], i32)
        first_n = sb("first_n", [P, 1], fp32)
        cont = sb("cont", [P, 2], fp32)
        diag = sb("diag", [P, 2, P], fp32)
        row_keep = sb("row_keep", [D, 2, P], fp32)
        row_limit = sb("row_limit", [D, 2, P], fp32)
        open_row = sb("open_row", [D, P + 1], fp32)
        carry_t = sb("carry_t", [D, P], fp32)
        fix_i = sb("fix_i", [P, 1], i32)
        fix = sb("fix", [P, D], fp32)
        count = sb("count", [HI, P], fp32)
        has_h = sb("has_h", [HI, P], fp32)
        total = sb("total", [HI, P], fp32)
        end_f = sb("end_f", [HI, P], fp32)
        end_i = sb("end_i", [HI, P], i32)

        ps_t = [pb(f"ps_t{i}", [P, 512]) for i in range(2)]
        ps_c = [pb(f"ps_c{i}", [P, 512]) for i in range(4)]
        ps_hist = pb("ps_hist", [P, 512])
        ps_m = pb("ps_m", [P, 512])
        ps_wt = ps_m[0:2 * D, 0:2 * D]
        ps_row = ps_m[0:D, 0:2 * P]
        ps_open = ps_m[0:D, 256:256 + P]
        ps_carry = ps_m[:, 384:384 + D]
        ps_off = ps_m[0:HI, 500:501]

        w_loaded = sem("w_loaded")
        x_loaded = sem("x_loaded")
        dst_loaded = sem("dst_loaded")
        small_loaded = sem("small_loaded")
        const_made = sem("const_made")
        x_pad = sem("x_pad")
        prep = sem("prep")
        w_turned = sem("w_turned")
        x_turned = sem("x_turned")
        xt_ready = sem("xt_ready")
        ca_ready = sem("ca_ready")
        ca_kept = sem("ca_kept")
        c_stored = sem("c_stored")
        rows_spread = sem("rows_spread")
        spread_kept = sem("spread_kept")
        hot_ready = sem("hot_ready")
        hot_used = sem("hot_used")
        hist_started = sem("hist_started")
        totals = sem("totals")
        offsets = sem("offsets")
        ends_made = sem("ends_made")
        ends_out = sem("ends_out")
        ends_back = sem("ends_back")
        idx_loaded = [sem(f"idx_loaded{s}") for s in range(2)]
        gather_begun = sem("gather_begun")
        gathered = [sem(f"gathered{s}") for s in range(2)]
        edge_loaded = [sem(f"edge_loaded{s}") for s in range(2)]
        edge_pad = sem("edge_pad")
        added = sem("added")
        relued = sem("relued")
        scanned = sem("scanned")
        scan_stored = [sem(f"scan_stored{s}") for s in range(2)]
        open_turned = sem("open_turned")
        open_scanned = sem("open_scanned")
        carry_made = sem("carry_made")
        carry_turned = sem("carry_turned")
        fix_loaded = sem("fix_loaded")
        fixed = sem("fixed")
        fix_stored = sem("fix_stored")
        node_rows = [sem(f"node_rows{g}") for g in range(len(NODE_GROUPS))]
        step = sem("step")
        centred = sem("centred")
        squared = sem("squared")
        var_made = sem("var_made")
        std_made = sem("std_made")
        normed = sem("normed")
        x1_stored = sem("x1_stored")
        out_stored = sem("out_stored")

        block = ctx.enter_context(nc.Block())

        PER_SLOT = CHUNKS // 2

        def rounds(layer, pair):
            return pair + (PER_SLOT * layer + 1)

        def at(layer, pair, slot):
            return pair * 2 + (CHUNKS * layer + slot)

        def rows_done(layer, pair, slot):
            steps_before = layer * (PAIRS * T + TAIL[slot])
            if isinstance(pair, int) and pair == PAIRS:
                return 16 * (steps_before + PAIRS * T + TAIL[slot])
            return pair * (16 * T) + 16 * (steps_before + T)

        @block.sync
        def _(sp):
            for h in range(2):
                sp.dma_start(theta2[:, h, :], theta_w).then_inc(w_loaded, 16)
                sp.dma_start(phi2[:, h, :], phi_w).then_inc(w_loaded, 16)
            sp.dma_start(x_sb[0:96, :, :], x_full[0:96]).then_inc(x_loaded, 16)
            sp.dma_start(bias[:, 0, :], phi_b.partition_broadcast(P)).then_inc(small_loaded, 16)
            sp.dma_start(bias[:, 1, :], theta_b.partition_broadcast(P)).then_inc(small_loaded, 16)
            sp.dma_start(eps1[:, :], eps.partition_broadcast(P)).then_inc(small_loaded, 16)
            sp.wait_ge(const_made, 6)
            with nc.allow_non_contiguous_dma(reason="one element of each partition"):
                sp.dma_start(prev[1:P, :], dst[0:P - 1, STEPS - 1:STEPS]).then_inc(small_loaded, 16)
            sp.dma_start(dst_sb[:, :], dst).then_inc(dst_loaded, 16)

            def load_idx(layer, pair, slot, t0, n):
                sp.dma_start(idx[:, slot, 0:n], src[:, bass.ds(t0, n)]).then_inc(idx_loaded[slot], 16)

            for slot in range(2):
                load_idx(0, 0, slot, slot * T, T)
            for a, b in zip(C_PARTS, C_PARTS[1:]):
                sp.wait_ge(ca_kept, 2 * b)
                k0, k1 = 8 * a, min(8 * b, K)
                sp.dma_start(c_tiles[:, k0:k1, :], rows_sb[:, k0:k1, :]).then_inc(c_stored, 16)

            with sp.Fori(1, PAIRS) as pair:
                for slot in range(2):
                    sp.wait_ge(scanned, at(0, pair, slot) - 1)
                    load_idx(0, pair, slot, pair * (2 * T) + slot * T, T)
            for slot in range(2):
                sp.wait_ge(scanned, at(0, PAIRS, slot) - 1)
                load_idx(0, PAIRS, slot, (MAIN + slot) * T, TAIL[slot])
            sp.wait_ge(ends_made, 2)
            sp.dma_start(end_dram, end_i[:, :]).then_inc(ends_out, 16)
            sp.dma_start(has_dram, has_h[:, :]).then_inc(ends_out, 16)
            sp.wait_ge(ends_out, 32)
            sp.dma_start(end_sb[:, :], end_tiles).then_inc(ends_back, 16)
            sp.dma_start(has_sb[:, :], has_tiles).then_inc(ends_back, 16)

            def load_chunk(pair, slot, t0):
                load_idx(1, pair, slot, t0, T)
                sp.dma_start(edge[:, slot, :], edge_all[:, bass.ds(t0 * D, T * D)])\
                  .then_inc(edge_loaded[slot], 16)

            for slot in range(2):
                sp.wait_ge(scanned, at(1, 0, slot) - 1)
                load_chunk(0, slot, slot * T)
            for g, (k0, n) in enumerate(zip(GROUP_AT, NODE_GROUPS)):
                sp.wait_ge(normed, g + 1)
                sp.dma_start(x1_tiles[:, k0:k0 + n, :], x1_sb[:, k0:k0 + n, :]).then_inc(x1_stored, 16)
            with sp.Fori(1, PAIRS) as pair:
                for slot in range(2):
                    sp.wait_ge(scanned, at(1, pair, slot) - 1)
                    load_chunk(pair, slot, pair * (2 * T) + slot * T)
            for slot in range(2):
                t0, n = (MAIN + slot) * T, TAIL[slot]
                sp.wait_ge(scanned, at(1, PAIRS, slot) - 1)
                load_idx(1, PAIRS, slot, t0, n)
                sp.wait_ge(edge_pad, slot + 1)
                for part in (FULL_LOW, FULL_HIGH):
                    sp.dma_start(edge[part, slot, 0:n * D], edge_full[part, t0 * D:(t0 + n) * D])\
                      .then_inc(edge_loaded[slot], 16)
                if t0 < LAST:
                    m = min(LAST - t0, n)
                    sp.dma_start(edge[P - 1:P, slot, 0:m * D], edge_last[:, t0 * D:(t0 + m) * D])\
                      .then_inc(edge_loaded[slot], 16)
            for g, (k0, n) in enumerate(zip(GROUP_AT, NODE_GROUPS)):
                sp.wait_ge(normed, len(NODE_GROUPS) + g + 1)
                for part in (FULL_LOW, FULL_HIGH):
                    sp.dma_start(out_full[part, k0:k0 + n, :], rows_sb[part, k0:k0 + n, :])\
                      .then_inc(out_stored, 16)
                if k0 < NLAST:
                    m = min(NLAST - k0, n)
                    first = (P - 1) * K + k0
                    sp.dma_start(out[first:first + m, :].rearrange("(p k) d -> p k d", p=1),
                                 rows_sb[P - 1:P, k0:k0 + m, :]).then_inc(out_stored, 16)
            sp.wait_ge(out_stored, 16 * sum(2 + (k0 < NLAST) for k0 in GROUP_AT))

        @block.scalar
        def _(act):
            act.wait_ge(x_pad, 1)
            act.dma_start(x_sb[96:112, :, :], x_full[96:112]).then_inc(x_loaded, 16)
            act.dma_start(x_sb[112:P - 1, :, :], x_full[112:P - 1]).then_inc(x_loaded, 16)
            act.dma_start(x_sb[P - 1:P, 0:NLAST, :],
                          x[(P - 1) * K:N, :].rearrange("(p k) d -> p k d", p=1)).then_inc(x_loaded, 16)
            for g, tiles in enumerate(PROD_GROUPS):
                act.wait_ge(x_turned, g + 1)
                if g >= 2:
                    act.wait_ge(ca_ready, g - 1)
                w = len(tiles) * P
                act.activation(xt[:, g % 2, 0:w], ps_t[g % 2][0:2 * D, 0:w], ACT.Copy).then_inc(xt_ready, 1)

            def store(layer, pair, slot, t0, n):
                act.wait_ge(scanned, at(layer, pair, slot) + 1)
                act.dma_start(scan_tiles[:, bass.ds(t0 * D, n * D)], scan[:, slot, 0:n * D])\
                   .then_inc(scan_stored[slot], 16)

            def relu(layer, pair, slot, n):
                act.wait_ge(added, at(0, pair, slot) + 1)
                act.activation(gath[:, slot, 0:n * D], gath[:, slot, 0:n * D], ACT.Relu).then_inc(relued, 1)

            def norm_parts(layer):
                for g, n in enumerate(NODE_GROUPS):
                    done = layer * len(NODE_GROUPS) + g + 1
                    k0 = GROUP_AT[g]
                    act.wait_ge(centred, done)
                    act.activation(square[:, 0:n, :], rows_sb[:, k0:k0 + n, :], ACT.Square).then_inc(squared, 1)
                    act.wait_ge(var_made, done)
                    act.activation(rstd[:, 0:n], rstd[:, 0:n], ACT.Sqrt, bias=eps_ln[:, :], scale=1.0 / D)\
                       .then_inc(std_made, 1)

            for layer in range(2):
                with act.Fori(0, PAIRS) as pair:
                    for slot in range(2):
                        if layer:
                            relu(layer, pair, slot, T)
                        store(layer, pair, slot, pair * (2 * T) + slot * T, T)
                for slot in range(2):
                    if layer:
                        relu(layer, PAIRS, slot, TAIL[slot])
                    store(layer, PAIRS, slot, (MAIN + slot) * T, TAIL[slot])
                if layer == 0:
                    act.wait_ge(const_made, 9)
                norm_parts(layer)

        @block.gpsimd
        def _(pool):
            pool.memset(ident[:, :], 0.0).then_inc(const_made, 1)
            pool.memset(ones[:, :], 1.0).then_inc(const_made, 1)
            pool.memset(before[:, :], 0.0).then_inc(const_made, 1)
            pool.memset(half[:, :], 1.0).then_inc(const_made, 1)
            pool.memset(prev[:, :], -1).then_inc(const_made, 1)
            pool.memset(zero_b[:, :], 0.0).then_inc(const_made, 1)
            pool.iota(lane_i[:, :], pattern=[[1, P]], base=0, channel_multiplier=0).then_inc(const_made, 1)
            pool.iota(part_end[:, :], pattern=[[0, 1]], base=-1, channel_multiplier=STEPS).then_inc(const_made, 1)
            pool.memset(eps_ln[:, :], EPS_LN).then_inc(const_made, 1)
            pool.wait_ge(const_made, 9)
            pool.affine_select(out=ident[:, :], in_=ident[:, :], compare_op=ALU.not_equal, fill=1.0,
                               base=0, pattern=[[-1, P]], channel_multiplier=1).then_inc(const_made, 1)
            pool.affine_select(out=half[:, 0:1], in_=half[:, 0:1], compare_op=ALU.is_ge, fill=0.0,
                               base=D - 1, pattern=[[0, 1]], channel_multiplier=-1).then_inc(const_made, 1)
            pool.affine_select(out=half[:, 1:2], in_=half[:, 1:2], compare_op=ALU.is_ge, fill=0.0,
                               base=-D, pattern=[[0, 1]], channel_multiplier=1).then_inc(const_made, 1)
            pool.affine_select(out=before[:, :], in_=before[:, :], compare_op=ALU.is_ge, fill=1.0,
                               base=0, pattern=[[-1, HI]], channel_multiplier=1).then_inc(const_made, 1)
            def gather(layer, pair, slot, n, first=False):
                pool.wait_ge(idx_loaded[slot], rounds(layer, pair) * 16)
                if not first:
                    pool.wait_ge(scanned, at(layer, pair, slot) - 1)
                table = (c_dram, x1_dram)[layer]
                pool.sem_inc(gather_begun, 1)
                for t in range(n):
                    pool.indirect_dma_start(
                        gath[:, slot, t * D:(t + 1) * D], None, table,
                        bass.IndirectOffsetOnAxis(ap=idx[:, slot, t:t + 1], axis=0),
                    ).then_inc(gathered[slot], 16)

            for layer in range(2):
                pool.wait_ge((c_stored, x1_stored)[layer], 16 * (len(C_PARTS) - 1, len(NODE_GROUPS))[layer])
                for slot in range(2):
                    gather(layer, 0, slot, T, first=layer == 0)
                with pool.Fori(1, PAIRS) as pair:
                    for slot in range(2):
                        gather(layer, pair, slot, T)
                for slot in range(2):
                    gather(layer, PAIRS, slot, TAIL[slot])
                for slot in range(2):
                    pool.wait_ge(scan_stored[slot], 16 * PER_SLOT * (layer + 1))
                if layer == 0:
                    pool.wait_ge(spread_kept, 3)
                pool.indirect_dma_start(fix[:, :], None, scan_dram,
                                        bass.IndirectOffsetOnAxis(ap=fix_i[:, :], axis=0)).then_inc(fix_loaded, 16)
                pool.wait_ge(fixed, layer + 1)
                pool.indirect_dma_start(scan_dram, bass.IndirectOffsetOnAxis(ap=fix_i[:, :], axis=0),
                                        fix[:, :], None).then_inc(fix_stored, 16)
                pool.wait_ge(fix_stored, 16 * (layer + 1))
                if layer == 0:
                    pool.wait_ge(ends_back, 32)
                for g, (k0, n) in enumerate(zip(GROUP_AT, NODE_GROUPS)):
                    for k in range(k0, k0 + n):
                        pool.indirect_dma_start(
                            rows_sb[:, k, :], None, scan_dram,
                            bass.IndirectOffsetOnAxis(ap=end_sb[:, k:k + 1], axis=0),
                        ).then_inc(node_rows[g], 16)

        @block.tensor
        def _(pe):
            pe.wait_ge(const_made, 13)
            pe.wait_ge(prep, 1)
            pe.transpose(ps_wt[:, 0:D], phi2[:, :, :].rearrange("o h i -> o (h i)"), ident[0:D, 0:D])
            pe.transpose(ps_wt[:, D:2 * D], theta2[:, :, :].rearrange("o h i -> o (h i)"),
                         ident[0:D, 0:D]).then_inc(w_turned, 1)

            def turn(g):
                if g >= 2:
                    pe.wait_ge(xt_ready, g - 1)
                for n, j in enumerate(PROD_GROUPS[g]):
                    mm = pe.transpose(ps_t[g % 2][0:2 * D, n * P:(n + 1) * P],
                                      x_sb[:, 2 * j:2 * j + 2, :].rearrange("p k d -> p (k d)"), ident[:, :])
                mm.then_inc(x_turned, 1)

            def product(g):
                if g == 0:
                    pe.wait_ge(prep, 2)
                pe.wait_ge(xt_ready, g + 1)
                if g >= 2:
                    pe.wait_ge(ca_kept, 2 * (g - 1))
                for n, j in enumerate(PROD_GROUPS[g]):
                    bank = ps_c[2 * (g % 2) + n // 2]
                    mm = pe.matmul(bank[:, (n % 2) * 4 * D:(n % 2 + 1) * 4 * D],
                                   xt[:, g % 2, n * P:(n + 1) * P],
                                   wt[:, :, :].rearrange("i h o -> i (h o)"), start=True, stop=True)
                mm.then_inc(ca_ready, 1)

            pe.wait_ge(x_loaded, 64)
            turn(0)
            for g in range(len(PROD_GROUPS)):
                if g + 1 < len(PROD_GROUPS):
                    turn(g + 1)
                product(g)
            pe.wait_ge(rows_spread, 1)
            pe.matmul(ps_row, ones[:, 0:D], diag[:, :, :].rearrange("p h n -> p (h n)"),
                      start=True, stop=True).then_inc(rows_spread, 1)

            pe.matmul(ps_hist[0:HI, 0:P], zero_b[:, 0:HI], zero_b[:, :], start=True, stop=False,
                      skip_group_check=True).then_inc(hist_started, 1)

            def count_batch(number, slot, n, last=False):
                pe.wait_ge(hot_ready, number + 1)
                for t in range(n):
                    mm = pe.matmul(ps_hist[0:HI, 0:P], hot_hi[:, slot, t, :], hot_lo[:, slot, t, :],
                                   start=False, stop=last and t == n - 1, skip_group_check=True)
                mm.then_inc(hot_used, 1)

            with pe.Fori(0, MAIN * BATCHES // 2) as two:
                for slot in range(2):
                    count_batch(two * 2 + slot, slot, B)
            for b, n in enumerate(TAIL_BATCHES):
                count_batch(MAIN * BATCHES + b, b % 2, n, last=b == len(TAIL_BATCHES) - 1)
            pe.wait_ge(totals, 1)
            pe.matmul(ps_off, before[:, :], total[:, P - 1:P], start=True, stop=True).then_inc(offsets, 1)

            for layer in range(2):
                pe.wait_ge(scanned, CHUNKS * (layer + 1))
                n = TAIL[1]
                pe.transpose(ps_open, scan[:, 1, (n - 1) * D:n * D], ident[:, :]).then_inc(open_turned, 1)
                pe.wait_ge(carry_made, layer + 1)
                pe.transpose(ps_carry, carry_t[:, :], ident[0:D, 0:D]).then_inc(carry_turned, 1)

        @block.vector
        def _(dve):
            dve.memset(x_sb[96:P, NLAST:K, :], 0.0).then_inc(x_pad, 1)
            dve.wait_ge(w_loaded, 64)
            dve.tensor_tensor(phi2[:, :, :], phi2[:, :, :], theta2[:, :, :], ALU.subtract).then_inc(prep, 1)
            dve.wait_ge(w_turned, 1)
            dve.wait_ge(const_made, 13)
            for h in range(2):
                w = dve.tensor_scalar(wt[:, h, :], ps_wt, half[:, h:h + 1], None, ALU.mult)
            w.then_inc(prep, 1)
            dve.wait_ge(small_loaded, 64)
            for g, tiles in enumerate(PROD_GROUPS):
                dve.wait_ge(ca_ready, g + 1)
                for part, kept in enumerate((rows_sb, a_sb)):
                    for b in range(0, len(tiles), 2):
                        k0, n = 2 * tiles[b], 2 * min(2, len(tiles) - b)
                        bank = ps_c[2 * (g % 2) + b // 2][:, 0:n * 2 * D]
                        made = bank.rearrange("p (k h d) -> p k h d", h=2, d=D)[:, :, part, :]
                        ins = dve.tensor_tensor(kept[:, k0:k0 + n, :], made,
                                                bias[:, part:part + 1, :].to_broadcast([P, n, D]), ALU.add)
                    ins.then_inc(ca_kept, 1)

            dve.wait_ge(dst_loaded, 16)
            dve.memset(keep[:, 0:1], 0.0)
            dve.tensor_tensor(keep[:, 1:STEPS], dst_sb[:, 1:STEPS], dst_sb[:, 0:STEPS - 1], ALU.is_equal)\
               .then_inc(prep, 1)
            dve.wait_ge(prep, 3)
            dve.tensor_scalar(limit[:, :], keep[:, :], 2.0, -1.0, ALU.mult, ALU.add).then_inc(prep, 1)
            dve.wait_ge(prep, 4)
            dve.tensor_scalar(limit[:, :], limit[:, :], HUGE, None, ALU.mult).then_inc(prep, 1)
            dve.tensor_scalar(scratch_i, dst_sb[:, :], 7, None, ALU.logical_shift_right).then_inc(prep, 1)
            dve.wait_ge(prep, 6)
            dve.tensor_copy(dst_hi[:, :], scratch_i).then_inc(prep, 1)
            dve.wait_ge(prep, 7)
            dve.tensor_scalar(scratch_i, dst_sb[:, :], 127, None, ALU.bitwise_and).then_inc(prep, 1)
            dve.wait_ge(prep, 8)
            dve.tensor_copy(dst_lo[:, :], scratch_i)
            dve.tensor_copy(lane[:, :], lane_i[:, :]).then_inc(prep, 1)
            dve.wait_ge(prep, 9)
            dve.tensor_tensor(scratch, dst_sb[:, :], dst_sb[:, 0:1].to_broadcast([P, STEPS]), ALU.is_equal)\
               .then_inc(prep, 1)
            dve.wait_ge(prep, 10)
            dve.tensor_reduce(first_n[:, :], scratch, AX.X, ALU.add)
            dve.tensor_tensor(cont[:, 0:1], prev[:, :], dst_sb[:, 0:1], ALU.is_equal).then_inc(prep, 1)
            dve.wait_ge(prep, 11)
            dve.tensor_scalar(cont[:, 1:2], first_n[:, :], float(STEPS), cont[:, 0:1], ALU.is_equal, ALU.mult)
            dve.tensor_tensor(fix_i[:, :], part_end[:, :], first_n[:, :], ALU.add).then_inc(prep, 1)
            dve.wait_ge(prep, 12)
            for h in range(2):
                ins = dve.tensor_scalar(diag[:, h, :], ident[:, :], cont[:, h:h + 1], None, ALU.mult)
            ins.then_inc(rows_spread, 1)
            dve.wait_ge(rows_spread, 2)
            dve.tensor_copy(row_keep[:, :, :], ps_row.rearrange("p (h n) -> p h n", h=2)).then_inc(spread_kept, 1)
            dve.wait_ge(spread_kept, 1)
            dve.tensor_scalar(row_limit[:, :, :], row_keep[:, :, :], 2.0, -1.0, ALU.mult, ALU.add)\
               .then_inc(spread_kept, 1)
            dve.wait_ge(spread_kept, 2)
            dve.tensor_scalar(row_limit[:, :, :], row_limit[:, :, :], HUGE, None, ALU.mult)
            dve.memset(open_row[:, 0:1], 0.0)
            dve.memset(scan[:, 1, (T - 1) * D:T * D], 0.0).then_inc(spread_kept, 1)

            def hot_batch(number, slot, t0, n, first=False):
                if not first:
                    dve.wait_ge(hot_used, number - 1)
                dve.tensor_tensor(
                    hot_lo[:, slot, 0:n, :], lane[:, :].unsqueeze(1).to_broadcast([P, n, P]),
                    dst_lo[:, bass.ds(t0, n)].unsqueeze(2).to_broadcast([P, n, P]), ALU.is_equal)
                dve.tensor_tensor(
                    hot_hi[:, slot, 0:n, :], lane[:, 0:HI].unsqueeze(1).to_broadcast([P, n, HI]),
                    dst_hi[:, bass.ds(t0, n)].unsqueeze(2).to_broadcast([P, n, HI]), ALU.is_equal)\
                   .then_inc(hot_ready, 1)

            def scan_chunk(layer, pair, slot, t0, n, stored_wait=True):
                if stored_wait:
                    dve.wait_ge(scan_stored[slot], (rounds(layer, pair) - 1) * 16)
                if isinstance(pair, int) and pair == 0 and slot == 0:
                    before_n = T
                    if layer == 0:
                        dve.wait_ge(spread_kept, 3)
                else:
                    before_n = TAIL[0] if isinstance(pair, int) and pair == PAIRS and slot else T
                    dve.wait_ge(scanned, at(layer, pair, slot))
                flow, op0, op1 = ((limit, ALU.min, ALU.max), (keep, ALU.mult, ALU.add))[layer]
                for f in range(D):
                    ins = dve.tensor_tensor_scan(
                        out=scan[:, slot, f:n * D:D], data0=flow[:, bass.ds(t0, n)],
                        data1=gath[:, slot, f:n * D:D],
                        initial=scan[:, 1 - slot, (before_n - 1) * D + f:(before_n - 1) * D + f + 1],
                        op0=op0, op1=op1)
                ins.then_inc(scanned, 1)

            def max_chunk(pair, slot, t0, n, first=False):
                dve.wait_ge(gathered[slot], rows_done(0, pair, slot))
                scan_chunk(0, pair, slot, t0, n, stored_wait=not first)

            def hot_chunk(pair, slot, t0, first=False):
                for b in range(BATCHES):
                    number = pair * (2 * BATCHES) + (slot * BATCHES + b)
                    hot_batch(number, b % 2, t0 + b * B, B, first=first and slot == 0 and b < 2)

            def sum_chunk(pair, slot, t0, n):
                dve.wait_ge(gathered[slot], rows_done(1, pair, slot))
                if isinstance(pair, int) and pair == PAIRS:
                    loads = 2 + (t0 < LAST)
                    dve.wait_ge(edge_loaded[slot], 16 * (PAIRS + loads))
                else:
                    dve.wait_ge(edge_loaded[slot], pair * 16 + 16)
                dve.tensor_tensor(gath[:, slot, 0:n * D], gath[:, slot, 0:n * D], edge[:, slot, 0:n * D],
                                  ALU.add).then_inc(added, 1)
                dve.wait_ge(relued, at(0, pair, slot) + 1)
                scan_chunk(1, pair, slot, t0, n)

            def carries(layer):
                flow = (row_limit, row_keep)[layer]
                op0, op1 = ((ALU.min, ALU.max), (ALU.mult, ALU.add))[layer]
                dve.wait_ge(open_turned, layer + 1)
                ins = dve.tensor_tensor_scan(out=open_row[:, 1:P + 1], data0=flow[:, 1, :], data1=ps_open,
                                             initial=0.0, op0=op0, op1=op1)
                ins.then_inc(open_scanned, 1)
                dve.wait_ge(open_scanned, layer + 1)
                dve.tensor_tensor(carry_t[:, :], open_row[:, 0:P], flow[:, 0, :], op0).then_inc(carry_made, 1)
                dve.wait_ge(carry_turned, layer + 1)
                dve.wait_ge(fix_loaded, 16 * (layer + 1))
                dve.tensor_tensor(fix[:, :], fix[:, :], ps_carry, op1).then_inc(fixed, 1)

            steps = [0]

            def chained(ins):
                steps[0] += 1
                ins.then_inc(step, 1)
                dve.wait_ge(step, steps[0])

            def node_stage(layer):
                for g, (k0, n) in enumerate(zip(GROUP_AT, NODE_GROUPS)):
                    done = layer * len(NODE_GROUPS) + g + 1
                    rows = rows_sb[:, k0:k0 + n, :]
                    has = has_sb[:, k0:k0 + n].unsqueeze(2).to_broadcast([P, n, D])
                    dve.wait_ge(node_rows[g], 16 * n * (layer + 1))
                    if layer == 0:
                        dve.wait_ge(ends_back, 32)
                        chained(dve.tensor_tensor(rows, rows, a_sb[:, k0:k0 + n, :], ALU.add))
                        chained(dve.tensor_tensor(rows, rows, has, ALU.mult))
                        chained(dve.tensor_tensor(rows, rows, x_sb[:, k0:k0 + n, :], ALU.add))
                    else:
                        chained(dve.tensor_tensor(rows, rows, has, ALU.mult))
                        chained(dve.scalar_tensor_tensor(out=rows, in0=x1_sb[:, k0:k0 + n, :],
                                                         scalar=eps1[:, 0:1], in1=rows,
                                                         op0=ALU.mult, op1=ALU.add))
                        chained(dve.tensor_tensor(rows, rows, x1_sb[:, k0:k0 + n, :], ALU.add))
                    chained(dve.tensor_reduce(mean[:, 0:n], rows, AX.X, ALU.add))
                    chained(dve.tensor_scalar(mean[:, 0:n], mean[:, 0:n], 1.0 / D, None, ALU.mult))
                    dve.tensor_tensor(rows, rows, mean[:, 0:n].unsqueeze(2).to_broadcast([P, n, D]),
                                      ALU.subtract).then_inc(centred, 1)
                    dve.wait_ge(squared, done)
                    dve.tensor_reduce(rstd[:, 0:n], square[:, 0:n, :], AX.X, ALU.add).then_inc(var_made, 1)
                    dve.wait_ge(std_made, done)
                    chained(dve.reciprocal(rstd[:, 0:n], rstd[:, 0:n]))
                    dve.tensor_tensor((x1_sb[:, k0:k0 + n, :], rows)[layer], rows,
                                      rstd[:, 0:n].unsqueeze(2).to_broadcast([P, n, D]), ALU.mult)\
                       .then_inc(normed, 1)

            for slot in range(2):
                hot_chunk(0, slot, slot * T, first=True)
                max_chunk(0, slot, slot * T, T, first=True)
            with dve.Fori(1, PAIRS) as pair:
                for slot in range(2):
                    hot_chunk(pair, slot, pair * (2 * T) + slot * T)
                    max_chunk(pair, slot, pair * (2 * T) + slot * T, T)
            for b, n in enumerate(TAIL_BATCHES):
                hot_batch(MAIN * BATCHES + b, b % 2, MAIN * T + b * B, n)
            dve.wait_ge(hot_used, MAIN * BATCHES + len(TAIL_BATCHES))
            chained(dve.tensor_copy(count[:, :], ps_hist[0:HI, 0:P]))
            dve.tensor_scalar(has_h[:, :], count[:, :], 1.0, None, ALU.min).then_inc(ends_made, 1)
            dve.tensor_tensor_scan(out=total[:, :], data0=ones[0:HI, :], data1=count[:, :], initial=0.0,
                                   op0=ALU.mult, op1=ALU.add).then_inc(totals, 1)
            dve.wait_ge(offsets, 1)
            dve.wait_ge(totals, 1)
            chained(dve.tensor_scalar(end_f[:, :], total[:, :], ps_off, -1.0, ALU.add, ALU.add))
            dve.tensor_scalar(end_i[:, :], end_f[:, :], 0.0, None, ALU.max).then_inc(ends_made, 1)
            chained(dve.tensor_scalar(eps1[:, :], eps1[:, :], 1.0, None, ALU.add))
            for slot in range(2):
                max_chunk(PAIRS, slot, (MAIN + slot) * T, TAIL[slot])
            carries(0)
            node_stage(0)

            for slot in range(2):
                sum_chunk(0, slot, slot * T, T)
            with dve.Fori(1, PAIRS) as pair:
                for slot in range(2):
                    sum_chunk(pair, slot, pair * (2 * T) + slot * T, T)
            for slot in range(2):
                dve.memset(edge[:, slot, :], 0.0).then_inc(edge_pad, 1)
            for slot in range(2):
                sum_chunk(PAIRS, slot, (MAIN + slot) * T, TAIL[slot])
            carries(1)
            node_stage(1)


_WEIGHTS = ['L0_gnn_theta_w', 'L0_gnn_theta_b', 'L0_gnn_phi_w', 'L0_gnn_phi_b', 'L1_gnn_eps']


def lay_out(inputs):
    import numpy as np
    x, edge_attr = (np.ascontiguousarray(inputs[n]) for n in ('x', 'edge_attr_48'))
    n_nodes, n_edges = x.shape[0], edge_attr.shape[0]
    steps = -(-n_edges // 128)
    pad = 128 * steps - n_edges
    arrays = {'x': x}
    for name, fill in (('src', 0), ('dst', n_nodes)):
        a = np.asarray(inputs[name])
        arrays[name] = np.concatenate([a, np.full(pad, fill, a.dtype)]).reshape(128, steps)
    arrays['edge_attr'] = edge_attr
    for name in _WEIGHTS:
        arrays[name] = np.ascontiguousarray(inputs[name])
    return arrays, (n_nodes, x.shape[1], n_edges)


def kernel(**inputs):
    import concourse.bacc as _bacc
    from concourse import mybir as _mybir
    from concourse.bass_utils import run_bass_kernel_spmd as _run

    arrays, shapes = lay_out(inputs)
    nc = _bacc.Bacc("TRN2", target_bir_lowering=False, num_devices=1)
    args = [nc.dram_tensor(name, list(a.shape), _mybir.dt.from_np(a.dtype), kind="ExternalInput").ap()
            for name, a in arrays.items()]
    out = nc.dram_tensor("out", [shapes[0], shapes[1]], _mybir.dt.float32, kind="ExternalOutput").ap()
    gnn_resnorm(nc, *args, out, shapes)
    return _run(nc, [arrays], core_ids=[0]).results[0]["out"]
```

```python
import concourse.bass as bass
from concourse import mybir
from contextlib import ExitStack


def gnn_resnorm(nc, x, src, dst, edge_attr, theta_w, theta_b, phi_w, phi_b, eps, out, shapes):
    fp32, bf16, i32 = mybir.dt.float32, mybir.dt.bfloat16, mybir.dt.int32
    ALU, ACT, AX = mybir.AluOpType, mybir.ActivationFunctionType, mybir.AxisListType

    N, D, E = shapes
    P = 128
    STEPS = -(-E // P)
    LAST = E - (P - 1) * STEPS
    T = 64
    PAIRS = LAST // (2 * T)
    MAIN = 2 * PAIRS
    SHORT = [16, 8]
    TAIL = [T, STEPS - (MAIN + 1) * T - sum(SHORT)] + SHORT
    TAIL_AT = [MAIN * T + sum(TAIL[:j]) for j in range(len(TAIL))]
    CHUNKS = MAIN + len(TAIL)
    FROM_X = 42
    assert 0 < TAIL[1] <= T and LAST > MAIN * T and CHUNKS % 2 == 0
    K = -(-N // P)
    NP = P * K
    NLAST = N - (P - 1) * K
    HI = NP // P
    B = 16
    BATCHES = T // B
    TAIL_STEPS = sum(TAIL)
    TAIL_BATCHES = [B] * (TAIL_STEPS // B) + ([TAIL_STEPS % B] if TAIL_STEPS % B else [])
    HUGE = 3.4028234e38
    EPS_LN = 1e-5
    NODE_GROUPS = [32, 32, 18, 10, K - 92]
    GMAX = max(NODE_GROUPS)
    GROUP_AT = [sum(NODE_GROUPS[:g]) for g in range(len(NODE_GROUPS))]
    PAIR_TILES = K // 2
    assert K % 2 == 0
    NODE_PRODS = [list(range(g, min(g + 4, PAIR_TILES))) for g in range(0, PAIR_TILES, 4)]
    STEP_PRODS = [list(range(g, min(g + 4, FROM_X // 2))) for g in range(0, FROM_X // 2, 4)]
    PRODS = [(False, g) for g in NODE_PRODS] + [(True, g) for g in STEP_PRODS]
    C_PARTS = [0, 4, 8, 11, len(NODE_PRODS)]
    BANK = 512
    FULL_LOW, FULL_HIGH = slice(0, 112), slice(112, P - 1)

    c_dram = nc.dram_tensor("c_rows", [NP, D], fp32).ap()
    x1_dram = nc.dram_tensor("x1_rows", [NP, D], fp32).ap()
    scan_dram = nc.dram_tensor("scan_rows", [P * STEPS, D], fp32).ap()
    end_dram = nc.dram_tensor("last_edge", [HI, P], i32).ap()
    has_dram = nc.dram_tensor("has_edges", [HI, P], fp32).ap()
    c_tiles = c_dram.rearrange("(p k) d -> p k d", k=K)
    x1_tiles = x1_dram.rearrange("(p k) d -> p k d", k=K)
    scan_tiles = scan_dram.rearrange("(p t) d -> p (t d)", t=STEPS)
    end_tiles = end_dram.rearrange("h l -> (h l)").rearrange("(p k) -> p k", k=K)
    has_tiles = has_dram.rearrange("h l -> (h l)").rearrange("(p k) -> p k", k=K)
    x_full = x[0:(P - 1) * K, :].rearrange("(p k) d -> p k d", k=K)
    out_full = out[0:(P - 1) * K, :].rearrange("(p k) d -> p k d", k=K)
    edge_full = edge_attr[0:(P - 1) * STEPS, :].rearrange("(p t) d -> p (t d)", t=STEPS)
    edge_last = edge_attr[(P - 1) * STEPS:E, :].rearrange("(p t) d -> p (t d)", p=1)
    edge_all = bass.AP(tensor=edge_attr.tensor, offset=0, ap=[[STEPS * D, P], [1, LAST * D]])

    with ExitStack() as ctx:
        def sb(name, shape, dt):
            return ctx.enter_context(nc.sbuf_tensor(name, shape, dt))

        def pb(name, shape, dt=fp32):
            return ctx.enter_context(nc.psum_tensor(name, shape, dt))

        def sem(name):
            return ctx.enter_context(nc.semaphore(name))

        x_sb = sb("x_sb", [P, K, D], fp32)
        a_sb = sb("a_sb", [P, K, D], fp32)
        rows_sb = sb("rows_sb", [P, K, D], fp32)
        x1_sb = sb("x1_sb", [P, K, D], fp32)
        square = sb("square", [P, GMAX, D], fp32)
        end_sb = sb("end_sb", [P, K], i32)
        has_sb = sb("has_sb", [P, K], fp32)
        mean = sb("mean", [P, GMAX], fp32)
        var = sb("var", [P, GMAX], fp32)
        rstd = sb("rstd", [P, GMAX], fp32)
        adjust = sb("adjust", [P, GMAX], fp32)
        idx = sb("idx", [P, 2, T], i32)
        gath = sb("gath", [P, 2, T * D], fp32)
        edge = sb("edge", [P, 2, T * D], fp32)
        scan = sb("scan", [P, 2, T * D], fp32)
        dst_sb = sb("dst_sb", [P, STEPS], i32)
        keep = sb("keep", [P, STEPS], fp32)
        dst_hi = sb("dst_hi", [P, STEPS], bf16)
        dst_lo = sb("dst_lo", [P, STEPS], bf16)
        scratch = edge[:, 0, 0:STEPS]
        scratch_i = scratch.bitcast(i32)
        hot_hi = sb("hot_hi", [P, 2, B, HI], bf16)
        hot_lo = sb("hot_lo", [P, 2, B, P], bf16)
        ident = sb("ident", [P, P], fp32)
        ones = sb("ones", [P, P], fp32)
        before = sb("before", [HI, HI], fp32)
        half = sb("half", [2 * D, 2], fp32)
        lane_i = sb("lane_i", [P, P], i32)
        zero_b = sb("zero_b", [P, P], bf16)
        part_end = sb("part_end", [P, 1], i32)
        eps1 = sb("eps1", [P, 1], fp32)
        theta2 = sb("theta2", [D, 2, D], fp32)
        phi2 = sb("phi2", [D, 2, D], fp32)
        wt = sb("wt", [2 * D, 2, 2 * D], fp32)
        bias = sb("bias", [P, 2, D], fp32)
        xt = sb("xt", [2 * D, 2, 4 * P], fp32)
        prev = sb("prev", [P, 1], i32)
        first_n = sb("first_n", [P, 1], fp32)
        cont = sb("cont", [P, 2], fp32)
        diag = sb("diag", [P, 2, P], fp32)
        row_keep = sb("row_keep", [D, 2, P], fp32)
        row_limit = sb("row_limit", [D, 2, P], fp32)
        open_row = sb("open_row", [D, P + 1], fp32)
        carry_t = sb("carry_t", [D, P], fp32)
        fix_i = sb("fix_i", [P, 1], i32)
        fix = sb("fix", [P, D], fp32)
        count = sb("count", [HI, P], fp32)
        has_h = sb("has_h", [HI, P], fp32)
        total = sb("total", [HI, P], fp32)
        end_f = sb("end_f", [HI, P], fp32)
        end_i = sb("end_i", [HI, P], i32)

        ps_t = [pb(f"ps_t{i}", [P, BANK]) for i in range(2)]
        ps_c = pb("ps_c", [P, 4 * BANK])
        ps_hist = pb("ps_hist", [P, BANK])
        ps_m = pb("ps_m", [P, BANK])
        assert STEPS <= 4 * BANK and BANK % T == 0
        flow = ps_c[:, 0:STEPS]
        lane = ps_t[1][:, 0:P]
        edge_ps = [ps_t[0], ps_hist]
        ps_wt = ps_m[0:2 * D, 0:2 * D]
        ps_row = ps_m[0:D, 0:2 * P]
        ps_open = ps_m[0:D, 256:256 + P]
        ps_carry = ps_m[:, 384:384 + D]
        ps_off = ps_m[0:HI, 500:501]

        w_loaded = sem("w_loaded")
        x_loaded = sem("x_loaded")
        dst_loaded = sem("dst_loaded")
        small_loaded = sem("small_loaded")
        const_made = sem("const_made")
        x_pad = sem("x_pad")
        prep = sem("prep")
        w_turned = sem("w_turned")
        x_turned = sem("x_turned")
        xt_ready = sem("xt_ready")
        ca_ready = sem("ca_ready")
        ca_kept = sem("ca_kept")
        c_stored = sem("c_stored")
        rows_spread = sem("rows_spread")
        spread_kept = sem("spread_kept")
        hot_ready = sem("hot_ready")
        hot_used = sem("hot_used")
        totals = sem("totals")
        offsets = sem("offsets")
        ends_made = sem("ends_made")
        ends_out = sem("ends_out")
        ends_back = sem("ends_back")
        idx_loaded = [sem(f"idx_loaded{s}") for s in range(2)]
        gather_begun = sem("gather_begun")
        first_gathered = sem("first_gathered")
        gathered = [sem(f"gathered{s}") for s in range(2)]
        edge_loaded = [sem(f"edge_loaded{s}") for s in range(2)]
        edge_pad = sem("edge_pad")
        edge_moved = sem("edge_moved")
        added = sem("added")
        relued = sem("relued")
        scanned = sem("scanned")
        row_scanned = sem("row_scanned")
        scan_stored = [sem(f"scan_stored{s}") for s in range(2)]
        open_turned = sem("open_turned")
        open_scanned = sem("open_scanned")
        carry_made = sem("carry_made")
        carry_turned = sem("carry_turned")
        fix_loaded = sem("fix_loaded")
        fixed = sem("fixed")
        fix_stored = sem("fix_stored")
        node_rows = [sem(f"node_rows{g}") for g in range(len(NODE_GROUPS))]
        step = sem("step")
        centred = sem("centred")
        squared = sem("squared")
        var_made = sem("var_made")
        std_made = sem("std_made")
        normed = sem("normed")
        x1_stored = sem("x1_stored")
        out_stored = sem("out_stored")

        block = ctx.enter_context(nc.Block())

        PER_SLOT = CHUNKS // 2

        def rounds(layer, pair):
            return pair + (PER_SLOT * layer + 1)

        def at(layer, pair, slot):
            return pair * 2 + (CHUNKS * layer + slot)

        def tail_number(pair, slot):
            return (pair - PAIRS) * 2 + slot if isinstance(pair, int) and pair >= PAIRS else None

        def rows_done(layer, pair, slot):
            before = layer * (PAIRS * T + sum(TAIL[slot::2])) - (0 if slot else FROM_X)
            j = tail_number(pair, slot)
            if j is not None:
                return 16 * (before + PAIRS * T + sum(TAIL[slot:j + 1:2]))
            return pair * (16 * T) + 16 * (before + T)

        PIECES = T * D // BANK
        assert T * D % BANK == 0

        def pieces(n):
            return [(a, min(a + BANK, n * D)) for a in range(0, n * D, BANK)]

        def piece_at(pair, slot):
            j = tail_number(pair, slot)
            if j is not None:
                return MAIN * PIECES + sum(len(pieces(n)) for n in TAIL[:j])
            return pair * (2 * PIECES) + slot * PIECES

        tail_chunks = [(PAIRS + j // 2, j % 2, t0, n) for j, (t0, n) in enumerate(zip(TAIL_AT, TAIL))]

        @block.sync
        def _(sp):
            def load_idx(layer, pair, slot, t0, n):
                sp.dma_start(idx[:, slot, 0:n], src[:, bass.ds(t0, n)]).then_inc(idx_loaded[slot], 16)

            load_idx(0, 0, 0, 0, T)
            for h in range(2):
                sp.dma_start(theta2[:, h, :], theta_w).then_inc(w_loaded, 16)
                sp.dma_start(phi2[:, h, :], phi_w).then_inc(w_loaded, 16)
            sp.dma_start(x_sb[0:96, :, :], x_full[0:96]).then_inc(x_loaded, 16)
            sp.dma_start(bias[:, 0, :], phi_b.partition_broadcast(P)).then_inc(small_loaded, 16)
            sp.dma_start(bias[:, 1, :], theta_b.partition_broadcast(P)).then_inc(small_loaded, 16)
            sp.dma_start(eps1[:, :], eps.partition_broadcast(P)).then_inc(small_loaded, 16)
            sp.wait_ge(const_made, 6)
            with nc.allow_non_contiguous_dma(reason="one element of each partition"):
                sp.dma_start(prev[1:P, :], dst[0:P - 1, STEPS - 1:STEPS]).then_inc(small_loaded, 16)
            sp.dma_start(dst_sb[:, :], dst).then_inc(dst_loaded, 16)

            load_idx(0, 0, 1, T, T)

            def load_edges(slot, t0):
                sp.dma_start(edge[:, slot, :], edge_all[:, bass.ds(t0 * D, T * D)])\
                  .then_inc(edge_loaded[slot], 16)

            for a, b in zip(C_PARTS, C_PARTS[1:]):
                sp.wait_ge(ca_kept, 2 * b)
                k0, k1 = 8 * a, min(8 * b, K)
                sp.dma_start(c_tiles[:, k0:k1, :], rows_sb[:, k0:k1, :]).then_inc(c_stored, 16)

            sp.wait_ge(spread_kept, 3)
            for slot in range(2):
                load_edges(slot, slot * T)

            with sp.Fori(1, PAIRS) as pair:
                for slot in range(2):
                    sp.wait_ge(scanned, at(0, pair, slot) - 1)
                    load_idx(0, pair, slot, pair * (2 * T) + slot * T, T)
            for pair, slot, t0, n in tail_chunks[:2]:
                sp.wait_ge(scanned, at(0, pair, slot) - 1)
                load_idx(0, pair, slot, t0, n)
            sp.wait_ge(ends_made, 2)
            sp.dma_start(end_dram, end_i[:, :]).then_inc(ends_out, 16)
            sp.dma_start(has_dram, has_h[:, :]).then_inc(ends_out, 16)
            sp.wait_ge(ends_out, 32)
            sp.dma_start(end_sb[:, :], end_tiles).then_inc(ends_back, 16)
            sp.dma_start(has_sb[:, :], has_tiles).then_inc(ends_back, 16)

            for pair, slot, t0, n in tail_chunks[2:]:
                sp.wait_ge(scanned, at(0, pair, slot) - 1)
                load_idx(0, pair, slot, t0, n)

            for slot in range(2):
                sp.wait_ge(scanned, at(1, 0, slot) - 1)
                load_idx(1, 0, slot, slot * T, T)
            for g, (k0, n) in enumerate(zip(GROUP_AT, NODE_GROUPS)):
                sp.wait_ge(normed, g + 1)
                sp.dma_start(x1_tiles[:, k0:k0 + n, :], x1_sb[:, k0:k0 + n, :]).then_inc(x1_stored, 16)
            with sp.Fori(1, PAIRS) as pair:
                for slot in range(2):
                    sp.wait_ge(scanned, at(1, pair, slot) - 1)
                    load_idx(1, pair, slot, pair * (2 * T) + slot * T, T)
                    load_edges(slot, pair * (2 * T) + slot * T)
            for pair, slot, t0, n in tail_chunks:
                sp.wait_ge(scanned, at(1, pair, slot) - 1)
                load_idx(1, pair, slot, t0, n)
                sp.wait_ge(edge_pad, slot + 1)
                for part in (FULL_LOW, FULL_HIGH):
                    sp.dma_start(edge[part, slot, 0:n * D], edge_full[part, t0 * D:(t0 + n) * D])\
                      .then_inc(edge_loaded[slot], 16)
                if t0 < LAST:
                    m = min(LAST - t0, n)
                    sp.dma_start(edge[P - 1:P, slot, 0:m * D], edge_last[:, t0 * D:(t0 + m) * D])\
                      .then_inc(edge_loaded[slot], 16)
            for g, (k0, n) in enumerate(zip(GROUP_AT, NODE_GROUPS)):
                sp.wait_ge(normed, len(NODE_GROUPS) + g + 1)
                for part in (FULL_LOW, FULL_HIGH):
                    sp.dma_start(out_full[part, k0:k0 + n, :], rows_sb[part, k0:k0 + n, :])\
                      .then_inc(out_stored, 16)
                if k0 < NLAST:
                    m = min(NLAST - k0, n)
                    first = (P - 1) * K + k0
                    sp.dma_start(out[first:first + m, :].rearrange("(p k) d -> p k d", p=1),
                                 rows_sb[P - 1:P, k0:k0 + m, :]).then_inc(out_stored, 16)
            sp.wait_ge(out_stored, 16 * sum(2 + (k0 < NLAST) for k0 in GROUP_AT))

        @block.scalar
        def _(act):
            act.wait_ge(x_pad, 1)
            act.dma_start(x_sb[96:112, :, :], x_full[96:112]).then_inc(x_loaded, 16)
            act.dma_start(x_sb[112:P - 1, :, :], x_full[112:P - 1]).then_inc(x_loaded, 16)
            act.dma_start(x_sb[P - 1:P, 0:NLAST, :],
                          x[(P - 1) * K:N, :].rearrange("(p k) d -> p k d", p=1)).then_inc(x_loaded, 16)
            for g, (_, tiles) in enumerate(PRODS):
                act.wait_ge(x_turned, g + 1)
                if g >= 2:
                    act.wait_ge(ca_ready, g - 1)
                w = len(tiles) * P
                act.activation(xt[:, g % 2, 0:w], ps_t[g % 2][0:2 * D, 0:w], ACT.Copy).then_inc(xt_ready, 1)

            def store(layer, pair, slot, t0, n):
                act.wait_ge(scanned, at(layer, pair, slot) + 1)
                act.dma_start(scan_tiles[:, bass.ds(t0 * D, n * D)], scan[:, slot, 0:n * D])\
                   .then_inc(scan_stored[slot], 16)

            def move_edges(pair, slot, n):
                j = tail_number(pair, slot)
                if j is None:
                    act.wait_ge(edge_loaded[slot], pair * 16 + 16)
                else:
                    loads = sum(2 + (t0 < LAST) for t0 in TAIL_AT[slot:j + 1:2])
                    act.wait_ge(edge_loaded[slot], 16 * (PAIRS + loads))
                if j is None and isinstance(pair, int) and slot == 0:
                    act.wait_ge(normed, len(NODE_GROUPS))
                for q, (a, b) in enumerate(pieces(n)):
                    if not (isinstance(pair, int) and pair == 0 and slot == 0 and q < 2):
                        act.wait_ge(added, piece_at(pair, slot) + (q - 1))
                    act.activation(edge_ps[q % 2][:, 0:b - a], edge[:, slot, a:b], ACT.Copy).then_inc(edge_moved, 1)

            def relu(pair, slot, n):
                act.wait_ge(added, piece_at(pair, slot) + len(pieces(n)))
                act.activation(gath[:, slot, 0:n * D], gath[:, slot, 0:n * D], ACT.Relu).then_inc(relued, 1)

            def norm_parts(layer):
                for g, n in enumerate(NODE_GROUPS):
                    done = layer * len(NODE_GROUPS) + g + 1
                    k0 = GROUP_AT[g]
                    act.wait_ge(centred, done)
                    act.activation(square[:, 0:n, :], rows_sb[:, k0:k0 + n, :], ACT.Square).then_inc(squared, 1)
                    act.wait_ge(var_made, done)
                    act.activation(rstd[:, 0:n], var[:, 0:n], ACT.Sqrt).then_inc(std_made, 1)

            def chunk(layer, pair, slot, t0, n):
                if layer == 1:
                    move_edges(pair, slot, n)
                    relu(pair, slot, n)
                store(layer, pair, slot, t0, n)

            for layer in range(2):
                for slot in range(2):
                    chunk(layer, 0, slot, slot * T, T)
                with act.Fori(1, PAIRS) as pair:
                    for slot in range(2):
                        chunk(layer, pair, slot, pair * (2 * T) + slot * T, T)
                for pair, slot, t0, n in tail_chunks:
                    chunk(layer, pair, slot, t0, n)
                norm_parts(layer)

        @block.gpsimd
        def _(pool):
            def from_table(table, slot, t, arrived):
                pool.indirect_dma_start(
                    gath[:, slot, t * D:(t + 1) * D], None, table,
                    bass.IndirectOffsetOnAxis(ap=idx[:, slot, t:t + 1], axis=0),
                ).then_inc(arrived, 16)

            pool.memset(ident[:, :], 0.0).then_inc(const_made, 1)
            pool.memset(ones[:, :], 1.0).then_inc(const_made, 1)
            pool.memset(before[:, :], 0.0).then_inc(const_made, 1)
            pool.memset(half[:, :], 1.0).then_inc(const_made, 1)
            pool.memset(prev[:, :], -1).then_inc(const_made, 1)
            pool.memset(zero_b[:, :], 0.0).then_inc(const_made, 1)
            pool.iota(lane_i[:, :], pattern=[[1, P]], base=0, channel_multiplier=0).then_inc(const_made, 1)
            pool.iota(part_end[:, :], pattern=[[0, 1]], base=-1, channel_multiplier=STEPS).then_inc(const_made, 1)
            pool.wait_ge(const_made, 8)
            pool.affine_select(out=ident[:, :], in_=ident[:, :], compare_op=ALU.not_equal, fill=1.0,
                               base=0, pattern=[[-1, P]], channel_multiplier=1).then_inc(const_made, 1)
            pool.affine_select(out=half[:, 0:1], in_=half[:, 0:1], compare_op=ALU.is_ge, fill=0.0,
                               base=D - 1, pattern=[[0, 1]], channel_multiplier=-1).then_inc(const_made, 1)
            pool.affine_select(out=half[:, 1:2], in_=half[:, 1:2], compare_op=ALU.is_ge, fill=0.0,
                               base=-D, pattern=[[0, 1]], channel_multiplier=1).then_inc(const_made, 1)
            pool.affine_select(out=before[:, :], in_=before[:, :], compare_op=ALU.is_ge, fill=1.0,
                               base=0, pattern=[[-1, HI]], channel_multiplier=1).then_inc(const_made, 1)
            pool.wait_ge(idx_loaded[0], 16)
            for t in range(FROM_X):
                from_table(x, 0, t, first_gathered)

            def gather(layer, pair, slot, n, first=False, t_first=0):
                pool.wait_ge(idx_loaded[slot], rounds(layer, pair) * 16)
                if not first:
                    pool.wait_ge(scanned, at(layer, pair, slot) - 1)
                pool.sem_inc(gather_begun, 1)
                for t in range(t_first, n):
                    from_table((c_dram, x1_dram)[layer], slot, t, gathered[slot])

            for layer in range(2):
                pool.wait_ge((c_stored, x1_stored)[layer], 16 * (len(C_PARTS) - 1, len(NODE_GROUPS))[layer])
                for slot in range(2):
                    gather(layer, 0, slot, T, first=layer == 0, t_first=FROM_X if (layer, slot) == (0, 0) else 0)
                with pool.Fori(1, PAIRS) as pair:
                    for slot in range(2):
                        gather(layer, pair, slot, T)
                for pair, slot, _, n in tail_chunks:
                    gather(layer, pair, slot, n)
                for slot in range(2):
                    pool.wait_ge(scan_stored[slot], 16 * PER_SLOT * (layer + 1))
                if layer == 0:
                    pool.wait_ge(spread_kept, 3)
                pool.indirect_dma_start(fix[:, :], None, scan_dram,
                                        bass.IndirectOffsetOnAxis(ap=fix_i[:, :], axis=0)).then_inc(fix_loaded, 16)
                pool.wait_ge(fixed, layer + 1)
                pool.indirect_dma_start(scan_dram, bass.IndirectOffsetOnAxis(ap=fix_i[:, :], axis=0),
                                        fix[:, :], None).then_inc(fix_stored, 16)
                pool.wait_ge(fix_stored, 16 * (layer + 1))
                if layer == 0:
                    pool.wait_ge(ends_back, 32)
                for g, (k0, n) in enumerate(zip(GROUP_AT, NODE_GROUPS)):
                    for k in range(k0, k0 + n):
                        pool.indirect_dma_start(
                            rows_sb[:, k, :], None, scan_dram,
                            bass.IndirectOffsetOnAxis(ap=end_sb[:, k:k + 1], axis=0),
                        ).then_inc(node_rows[g], 16)

        @block.tensor
        def _(pe):
            pe.wait_ge(const_made, 12)
            pe.wait_ge(prep, 1)
            pe.transpose(ps_wt[:, 0:D], phi2[:, :, :].rearrange("o h i -> o (h i)"), ident[0:D, 0:D])
            pe.transpose(ps_wt[:, D:2 * D], theta2[:, :, :].rearrange("o h i -> o (h i)"),
                         ident[0:D, 0:D]).then_inc(w_turned, 1)

            def turn(g):
                if g >= 2:
                    pe.wait_ge(xt_ready, g - 1)
                steps, tiles = PRODS[g]
                if steps:
                    pe.wait_ge(first_gathered, 16 * FROM_X)
                for n, j in enumerate(tiles):
                    rows = (gath[:, 0, 2 * j * D:(2 * j + 2) * D] if steps
                            else x_sb[:, 2 * j:2 * j + 2, :].rearrange("p k d -> p (k d)"))
                    mm = pe.transpose(ps_t[g % 2][0:2 * D, n * P:(n + 1) * P], rows, ident[:, :])
                mm.then_inc(x_turned, 1)

            def product(g):
                if g == 0:
                    pe.wait_ge(prep, 2)
                pe.wait_ge(xt_ready, g + 1)
                if g >= 2:
                    pe.wait_ge(ca_kept, 2 * (g - 1))
                for n in range(len(PRODS[g][1])):
                    column = (2 * (g % 2) + n // 2) * BANK + (n % 2) * 4 * D
                    mm = pe.matmul(ps_c[:, column:column + 4 * D],
                                   xt[:, g % 2, n * P:(n + 1) * P],
                                   wt[:, :, :].rearrange("i h o -> i (h o)"), start=True, stop=True)
                mm.then_inc(ca_ready, 1)

            pe.wait_ge(x_loaded, 64)
            turn(0)
            for g in range(len(PRODS)):
                ahead = g + 1 < len(PRODS) and PRODS[g + 1][0] == PRODS[g][0]
                if ahead:
                    turn(g + 1)
                product(g)
                if g + 1 < len(PRODS) and not ahead:
                    turn(g + 1)
            pe.wait_ge(rows_spread, 1)
            pe.matmul(ps_row, ones[:, 0:D], diag[:, :, :].rearrange("p h n -> p (h n)"),
                      start=True, stop=True).then_inc(rows_spread, 1)

            pe.matmul(ps_hist[0:HI, 0:P], zero_b[:, 0:HI], zero_b[:, :], start=True, stop=False,
                      skip_group_check=True)

            def count_batch(number, slot, n, last=False):
                pe.wait_ge(hot_ready, number + 1)
                for t in range(n):
                    mm = pe.matmul(ps_hist[0:HI, 0:P], hot_hi[:, slot, t, :], hot_lo[:, slot, t, :],
                                   start=False, stop=last and t == n - 1, skip_group_check=True)
                mm.then_inc(hot_used, 1)

            with pe.Fori(0, MAIN * BATCHES // 2) as two:
                for slot in range(2):
                    count_batch(two * 2 + slot, slot, B)
            for b, n in enumerate(TAIL_BATCHES):
                count_batch(MAIN * BATCHES + b, b % 2, n, last=b == len(TAIL_BATCHES) - 1)
            pe.wait_ge(totals, 1)
            pe.matmul(ps_off, before[:, :], total[:, P - 1:P], start=True, stop=True).then_inc(offsets, 1)

            for layer in range(2):
                pe.wait_ge(scanned, CHUNKS * (layer + 1))
                n = TAIL[-1]
                pe.transpose(ps_open, scan[:, 1, (n - 1) * D:n * D], ident[:, :]).then_inc(open_turned, 1)
                pe.wait_ge(carry_made, layer + 1)
                pe.transpose(ps_carry, carry_t[:, :], ident[0:D, 0:D]).then_inc(carry_turned, 1)

        @block.vector
        def _(dve):
            dve.memset(x_sb[96:P, NLAST:K, :], 0.0).then_inc(x_pad, 1)
            dve.wait_ge(w_loaded, 64)
            dve.tensor_tensor(phi2[:, :, :], phi2[:, :, :], theta2[:, :, :], ALU.subtract).then_inc(prep, 1)
            dve.wait_ge(w_turned, 1)
            dve.wait_ge(const_made, 12)
            for h in range(2):
                w = dve.tensor_scalar(wt[:, h, :], ps_wt, half[:, h:h + 1], None, ALU.mult)
            w.then_inc(prep, 1)
            dve.wait_ge(small_loaded, 64)
            first_rows = gath[:, 0, :].rearrange("p (t d) -> p t d", d=D)
            for g, (steps, tiles) in enumerate(PRODS):
                dve.wait_ge(ca_ready, g + 1)
                for part, kept in ((0, first_rows),) if steps else ((0, rows_sb), (1, a_sb)):
                    for b in range(0, len(tiles), 2):
                        k0, n = 2 * tiles[b], 2 * min(2, len(tiles) - b)
                        column = (2 * (g % 2) + b // 2) * BANK
                        made = ps_c[:, column:column + n * 2 * D]\
                            .rearrange("p (k h d) -> p k h d", h=2, d=D)[:, :, part, :]
                        ins = dve.tensor_tensor(kept[:, k0:k0 + n, :], made,
                                                bias[:, part:part + 1, :].to_broadcast([P, n, D]), ALU.add)
                    ins.then_inc(ca_kept, 2 if steps else 1)

            dve.wait_ge(dst_loaded, 16)
            dve.memset(keep[:, 0:1], 0.0)
            dve.tensor_tensor(keep[:, 1:STEPS], dst_sb[:, 1:STEPS], dst_sb[:, 0:STEPS - 1], ALU.is_equal)\
               .then_inc(prep, 1)
            dve.wait_ge(prep, 3)
            flow_parts = [(a, min(a + BANK, STEPS)) for a in range(0, STEPS, BANK)]
            for a, b in flow_parts:
                ins = dve.tensor_scalar(flow[:, a:b], keep[:, a:b], 2.0, -1.0, ALU.mult, ALU.add)
            ins.then_inc(prep, 1)
            dve.wait_ge(prep, 4)
            for a, b in flow_parts:
                ins = dve.tensor_scalar(flow[:, a:b], flow[:, a:b], HUGE, None, ALU.mult)
            ins.then_inc(prep, 1)
            dve.tensor_scalar(scratch_i, dst_sb[:, :], 7, None, ALU.logical_shift_right).then_inc(prep, 1)
            dve.wait_ge(prep, 6)
            dve.tensor_copy(dst_hi[:, :], scratch_i).then_inc(prep, 1)
            dve.wait_ge(prep, 7)
            dve.tensor_scalar(scratch_i, dst_sb[:, :], 127, None, ALU.bitwise_and).then_inc(prep, 1)
            dve.wait_ge(prep, 8)
            dve.tensor_copy(dst_lo[:, :], scratch_i)
            dve.tensor_copy(lane, lane_i[:, :]).then_inc(prep, 1)
            dve.wait_ge(prep, 9)
            dve.tensor_tensor(scratch, dst_sb[:, :], dst_sb[:, 0:1].to_broadcast([P, STEPS]), ALU.is_equal)\
               .then_inc(prep, 1)
            dve.wait_ge(prep, 10)
            dve.tensor_reduce(first_n[:, :], scratch, AX.X, ALU.add)
            dve.tensor_tensor(cont[:, 0:1], prev[:, :], dst_sb[:, 0:1], ALU.is_equal).then_inc(prep, 1)
            dve.wait_ge(prep, 11)
            dve.tensor_scalar(cont[:, 1:2], first_n[:, :], float(STEPS), cont[:, 0:1], ALU.is_equal, ALU.mult)
            dve.tensor_tensor(fix_i[:, :], part_end[:, :], first_n[:, :], ALU.add).then_inc(prep, 1)
            dve.wait_ge(prep, 12)
            for h in range(2):
                ins = dve.tensor_scalar(diag[:, h, :], ident[:, :], cont[:, h:h + 1], None, ALU.mult)
            ins.then_inc(rows_spread, 1)
            dve.wait_ge(rows_spread, 2)
            dve.tensor_copy(row_keep[:, :, :], ps_row.rearrange("p (h n) -> p h n", h=2)).then_inc(spread_kept, 1)
            dve.wait_ge(spread_kept, 1)
            dve.tensor_scalar(row_limit[:, :, :], row_keep[:, :, :], 2.0, -1.0, ALU.mult, ALU.add)\
               .then_inc(spread_kept, 1)
            dve.wait_ge(spread_kept, 2)
            dve.tensor_scalar(row_limit[:, :, :], row_limit[:, :, :], HUGE, None, ALU.mult)
            dve.memset(open_row[:, 0:1], 0.0)
            dve.memset(scan[:, 1, (T - 1) * D:T * D], 0.0).then_inc(spread_kept, 1)

            def hot_batch(number, slot, t0, n, first=False):
                if not first:
                    dve.wait_ge(hot_used, number - 1)
                dve.tensor_tensor(
                    hot_lo[:, slot, 0:n, :], lane.unsqueeze(1).to_broadcast([P, n, P]),
                    dst_lo[:, bass.ds(t0, n)].unsqueeze(2).to_broadcast([P, n, P]), ALU.is_equal)
                dve.tensor_tensor(
                    hot_hi[:, slot, 0:n, :], lane[:, 0:HI].unsqueeze(1).to_broadcast([P, n, HI]),
                    dst_hi[:, bass.ds(t0, n)].unsqueeze(2).to_broadcast([P, n, HI]), ALU.is_equal)\
                   .then_inc(hot_ready, 1)

            def scan_chunk(layer, pair, slot, t0, n, stored_wait=True):
                if stored_wait:
                    dve.wait_ge(scan_stored[slot], (rounds(layer, pair) - 1) * 16)
                j = tail_number(pair, slot)
                before_n = TAIL[j - 1] if j else T
                if layer == 0 and isinstance(pair, int) and pair == 0 and slot == 0:
                    dve.wait_ge(spread_kept, 3)
                else:
                    dve.wait_ge(scanned, at(layer, pair, slot))
                op0, op1 = ((ALU.min, ALU.max), (ALU.mult, ALU.add))[layer]
                if n in SHORT:
                    rows_before = layer * sum(m - 1 for m in SHORT) + sum(m - 1 for m in TAIL[2:j])
                    for t in range(n):
                        if t:
                            dve.wait_ge(row_scanned, rows_before + t)
                        row = scan[:, slot, (t - 1) * D:t * D] if t else \
                            scan[:, 1 - slot, (before_n - 1) * D:before_n * D]
                        dve.scalar_tensor_tensor(
                            out=scan[:, slot, t * D:(t + 1) * D], in0=row, scalar=flow[:, t0 + t:t0 + t + 1],
                            in1=gath[:, slot, t * D:(t + 1) * D], op0=op0, op1=op1,
                        ).then_inc(row_scanned if t < n - 1 else scanned, 1)
                    return
                for f in range(D):
                    ins = dve.tensor_tensor_scan(
                        out=scan[:, slot, f:n * D:D], data0=flow[:, bass.ds(t0, n)],
                        data1=gath[:, slot, f:n * D:D],
                        initial=scan[:, 1 - slot, (before_n - 1) * D + f:(before_n - 1) * D + f + 1],
                        op0=op0, op1=op1)
                ins.then_inc(scanned, 1)

            def max_chunk(pair, slot, t0, n, first=False):
                dve.wait_ge(gathered[slot], rows_done(0, pair, slot))
                scan_chunk(0, pair, slot, t0, n, stored_wait=not first)

            def hot_chunk(pair, slot, t0, first=False):
                for b in range(BATCHES):
                    number = pair * (2 * BATCHES) + (slot * BATCHES + b)
                    hot_batch(number, b % 2, t0 + b * B, B, first=first and slot == 0 and b < 2)

            def sum_chunk(pair, slot, t0, n):
                dve.wait_ge(gathered[slot], rows_done(1, pair, slot))
                for q, (a, b) in enumerate(pieces(n)):
                    dve.wait_ge(edge_moved, piece_at(pair, slot) + (q + 1))
                    dve.tensor_tensor(gath[:, slot, a:b], edge_ps[q % 2][:, 0:b - a], gath[:, slot, a:b],
                                      ALU.add).then_inc(added, 1)
                dve.wait_ge(relued, at(0, pair, slot) + 1)
                scan_chunk(1, pair, slot, t0, n)

            def carries(layer):
                over = (row_limit, row_keep)[layer]
                op0, op1 = ((ALU.min, ALU.max), (ALU.mult, ALU.add))[layer]
                dve.wait_ge(open_turned, layer + 1)
                ins = dve.tensor_tensor_scan(out=open_row[:, 1:P + 1], data0=over[:, 1, :], data1=ps_open,
                                             initial=0.0, op0=op0, op1=op1)
                ins.then_inc(open_scanned, 1)
                dve.wait_ge(open_scanned, layer + 1)
                dve.tensor_tensor(carry_t[:, :], open_row[:, 0:P], over[:, 0, :], op0).then_inc(carry_made, 1)
                dve.wait_ge(carry_turned, layer + 1)
                dve.wait_ge(fix_loaded, 16 * (layer + 1))
                dve.tensor_tensor(fix[:, :], fix[:, :], ps_carry, op1).then_inc(fixed, 1)

            steps = [0]

            def chained(ins):
                steps[0] += 1
                ins.then_inc(step, 1)
                dve.wait_ge(step, steps[0])

            def node_stage(layer):
                for g, (k0, n) in enumerate(zip(GROUP_AT, NODE_GROUPS)):
                    done = layer * len(NODE_GROUPS) + g + 1
                    rows = rows_sb[:, k0:k0 + n, :]
                    has = has_sb[:, k0:k0 + n].unsqueeze(2).to_broadcast([P, n, D])
                    dve.wait_ge(node_rows[g], 16 * n * (layer + 1))
                    if layer == 0:
                        dve.wait_ge(ends_back, 32)
                        chained(dve.tensor_tensor(rows, rows, a_sb[:, k0:k0 + n, :], ALU.add))
                        chained(dve.tensor_tensor(rows, rows, has, ALU.mult))
                        chained(dve.tensor_tensor(rows, rows, x_sb[:, k0:k0 + n, :], ALU.add))
                    else:
                        chained(dve.tensor_tensor(rows, rows, has, ALU.mult))
                        chained(dve.scalar_tensor_tensor(out=rows, in0=x1_sb[:, k0:k0 + n, :],
                                                         scalar=eps1[:, 0:1], in1=rows,
                                                         op0=ALU.mult, op1=ALU.add))
                        chained(dve.tensor_tensor(rows, rows, x1_sb[:, k0:k0 + n, :], ALU.add))
                    chained(dve.tensor_reduce(mean[:, 0:n], rows, AX.X, ALU.add))
                    chained(dve.tensor_scalar(mean[:, 0:n], mean[:, 0:n], 1.0 / D, None, ALU.mult))
                    dve.tensor_tensor(rows, rows, mean[:, 0:n].unsqueeze(2).to_broadcast([P, n, D]),
                                      ALU.subtract).then_inc(centred, 1)
                    dve.wait_ge(squared, done)
                    chained(dve.tensor_reduce(var[:, 0:n], square[:, 0:n, :], AX.X, ALU.add))
                    dve.tensor_scalar(var[:, 0:n], var[:, 0:n], 1.0 / D, EPS_LN, ALU.mult, ALU.add)\
                       .then_inc(var_made, 1)
                    dve.wait_ge(std_made, done)
                    chained(dve.reciprocal(rstd[:, 0:n], rstd[:, 0:n]))
                    chained(dve.scalar_tensor_tensor(out=adjust[:, 0:n], in0=rstd[:, 0:n], scalar=-0.5,
                                                     in1=rstd[:, 0:n], op0=ALU.mult, op1=ALU.mult))
                    chained(dve.tensor_tensor(adjust[:, 0:n], adjust[:, 0:n], var[:, 0:n], ALU.mult))
                    chained(dve.scalar_tensor_tensor(out=rstd[:, 0:n], in0=adjust[:, 0:n], scalar=1.5,
                                                     in1=rstd[:, 0:n], op0=ALU.add, op1=ALU.mult))
                    dve.tensor_tensor((x1_sb[:, k0:k0 + n, :], rows)[layer], rows,
                                      rstd[:, 0:n].unsqueeze(2).to_broadcast([P, n, D]), ALU.mult)\
                       .then_inc(normed, 1)

            for slot in range(2):
                hot_chunk(0, slot, slot * T, first=True)
                max_chunk(0, slot, slot * T, T, first=True)
            with dve.Fori(1, PAIRS) as pair:
                for slot in range(2):
                    hot_chunk(pair, slot, pair * (2 * T) + slot * T)
                    max_chunk(pair, slot, pair * (2 * T) + slot * T, T)
            for b, n in enumerate(TAIL_BATCHES):
                hot_batch(MAIN * BATCHES + b, b % 2, MAIN * T + b * B, n)
            dve.wait_ge(hot_used, MAIN * BATCHES + len(TAIL_BATCHES))
            chained(dve.tensor_copy(count[:, :], ps_hist[0:HI, 0:P]))
            dve.tensor_scalar(has_h[:, :], count[:, :], 1.0, None, ALU.min).then_inc(ends_made, 1)
            dve.tensor_tensor_scan(out=total[:, :], data0=ones[0:HI, :], data1=count[:, :], initial=0.0,
                                   op0=ALU.mult, op1=ALU.add).then_inc(totals, 1)
            dve.wait_ge(offsets, 1)
            chained(dve.tensor_scalar(end_f[:, :], total[:, :], ps_off, -1.0, ALU.add, ALU.add))
            dve.tensor_scalar(end_i[:, :], end_f[:, :], 0.0, None, ALU.max).then_inc(ends_made, 1)
            chained(dve.tensor_scalar(eps1[:, :], eps1[:, :], 1.0, None, ALU.add))
            for pair, slot, t0, n in tail_chunks:
                max_chunk(pair, slot, t0, n)
            dve.wait_ge(scanned, CHUNKS)
            carries(0)
            for a, b in flow_parts:
                ins = dve.tensor_copy(flow[:, a:b], keep[:, a:b])
            chained(ins)
            node_stage(0)

            for slot in range(2):
                sum_chunk(0, slot, slot * T, T)
            with dve.Fori(1, PAIRS) as pair:
                for slot in range(2):
                    sum_chunk(pair, slot, pair * (2 * T) + slot * T, T)
            for slot in range(2):
                dve.memset(edge[:, slot, :], 0.0).then_inc(edge_pad, 1)
            for pair, slot, t0, n in tail_chunks:
                sum_chunk(pair, slot, t0, n)
            carries(1)
            node_stage(1)


_WEIGHTS = ['L0_gnn_theta_w', 'L0_gnn_theta_b', 'L0_gnn_phi_w', 'L0_gnn_phi_b', 'L1_gnn_eps']


def lay_out(inputs):
    import numpy as np
    x, edge_attr = (np.ascontiguousarray(inputs[n]) for n in ('x', 'edge_attr_48'))
    n_nodes, n_edges = x.shape[0], edge_attr.shape[0]
    steps = -(-n_edges // 128)
    pad = 128 * steps - n_edges
    arrays = {'x': x}
    for name, fill in (('src', 0), ('dst', n_nodes)):
        a = np.asarray(inputs[name])
        arrays[name] = np.concatenate([a, np.full(pad, fill, a.dtype)]).reshape(128, steps)
    arrays['edge_attr'] = edge_attr
    for name in _WEIGHTS:
        arrays[name] = np.ascontiguousarray(inputs[name])
    return arrays, (n_nodes, x.shape[1], n_edges)


def kernel(**inputs):
    import concourse.bacc as _bacc
    from concourse import mybir as _mybir
    from concourse.bass_utils import run_bass_kernel_spmd as _run

    arrays, shapes = lay_out(inputs)
    nc = _bacc.Bacc("TRN2", target_bir_lowering=False, num_devices=1)
    args = [nc.dram_tensor(name, list(a.shape), _mybir.dt.from_np(a.dtype), kind="ExternalInput").ap()
            for name, a in arrays.items()]
    out = nc.dram_tensor("out", [shapes[0], shapes[1]], _mybir.dt.float32, kind="ExternalOutput").ap()
    gnn_resnorm(nc, *args, out, shapes)
    return _run(nc, [arrays], core_ids=[0]).results[0]["out"]
```
